# Optimizing a Trainium2 kernel written in Bass

```python
import numpy as np
import jax
import jax.numpy as jnp

def _softmax(x, axis=-1):
    return jax.nn.softmax(x, axis=axis)

def _gelu(x):
    return jax.nn.gelu(x, approximate=True)

def _silu(x):
    return jax.nn.silu(x)

def _sigmoid(x):
    return jax.nn.sigmoid(x)

def _layernorm(x, axis=-1, eps=1e-05):
    m = jnp.mean(x, axis=axis, keepdims=True)
    v = jnp.var(x, axis=axis, keepdims=True)
    return (x - m) / jnp.sqrt(v + eps)

def _scatter_add(tgt, idx, src, axis=0):
    return tgt.at[idx].add(src)

def _segment_sum(src, seg, n):
    return jax.ops.segment_sum(src, seg, n)
kernel_name = 'mk_gnn_preln_d4_gnn_r32_c0b34f'

def setup_inputs(seed: int=0):
    np.random.seed(seed)
    _w = jnp.asarray

    def _rec_inputs():
        import jax
        import jax.numpy as jnp
        _gk = jax.random.key(seed)
        x = -0.0003713 + 1 * jax.random.normal(jax.random.fold_in(_gk, 1), (50000, 128), jnp.float32)
        src = jax.random.randint(jax.random.fold_in(_gk, 2), (50000,), 0, 50000, jnp.int32)
        dst = jnp.minimum((50000 * jax.random.uniform(jax.random.fold_in(_gk, 3), (50000,)) ** 2.0).astype(jnp.int32), 49999)
        _o = jnp.argsort(dst, stable=True)
        src = src[_o]
        dst = dst[_o]
        edge_attr_3 = -0.000451519 + 1.00018 * jax.random.normal(jax.random.fold_in(_gk, 12), (50000, 3), jnp.float32)
        edge_weight = jax.random.uniform(jax.random.fold_in(_gk, 14), (50000,), jnp.float32, 0.0, 0.999998)
        return (x, src, dst, edge_attr_3, edge_weight)
    x, src, dst, edge_attr_3, edge_weight = _rec_inputs()

    def _L0_gnn_setup():
        import jax, jax.numpy as jnp
        import numpy as np
        N_NODES = 3125
        N_EDGES = 50000
        D_IN = 128
        D_OUT = 128
        key = jax.random.key(seed)
        k1, k2, k3, k4 = jax.random.split(key, 4)
        h = jax.random.normal(k1, (N_NODES, D_IN), dtype=jnp.float32)
        src = jax.random.randint(k2, (N_EDGES,), 0, N_NODES, dtype=jnp.int64 if jax.config.jax_enable_x64 else jnp.int32)
        dst = jax.random.randint(k3, (N_EDGES,), 0, N_NODES, dtype=jnp.int64 if jax.config.jax_enable_x64 else jnp.int32)
        W = jax.random.normal(k4, (D_OUT, 2 * D_IN), dtype=jnp.float32) * (1.0 / np.sqrt(2 * D_IN))
        b = jnp.zeros((D_OUT,), dtype=jnp.float32)
        return {'h': h, 'src': src, 'dst': dst, 'W': W, 'b': b}
    _L0_gnn_all = _L0_gnn_setup()
    _L0_gnn_in = {k: v for k, v in _L0_gnn_all.items() if k in ('W', 'b')}
    del _L0_gnn_all

    def _L1_gnn_setup():
        import jax, jax.numpy as jnp
        import numpy as np
        N = 50000
        E = 25000
        MUL = 32
        NB = 8
        R_MAX = 1.0
        AVG = 16.0
        SQ3 = 3.0 ** 0.5

        def _radial_embedding(r):
            x = jnp.clip(r / R_MAX, 0.0, 1.0)
            centers = jnp.arange(NB, dtype=jnp.float32) / (NB - 1)
            sigma = 1.0 / (NB - 1)
            emb = jnp.exp(-0.5 * ((x[:, None] - centers[None, :]) / sigma) ** 2)
            emb = emb * NB ** 0.5 * (r <= R_MAX).astype(jnp.float32)[:, None]
            return emb
        key = jax.random.key(seed)
        k = jax.random.split(key, 12)
        inp = {'node_feats': jax.random.normal(k[0], (N, 4 * MUL), dtype=jnp.float32), 'edge_vec': jax.random.normal(k[1], (E, 3), dtype=jnp.float32), 'edge_length': jax.random.uniform(k[2], (E,), dtype=jnp.float32), 'senders': jax.random.randint(k[3], (E,), 0, N, dtype=jnp.int32), 'receivers': jax.random.randint(k[4], (E,), 0, N, dtype=jnp.int32), 'num_nodes': N, 'W_up0': jax.random.normal(k[5], (MUL, MUL), dtype=jnp.float32), 'W_up1': jax.random.normal(k[6], (MUL, MUL), dtype=jnp.float32), 'mlp_w0': jax.random.normal(k[7], (NB, 64), dtype=jnp.float32) / NB ** 0.5, 'mlp_b0': jnp.zeros((64,), dtype=jnp.float32), 'mlp_w1': jax.random.normal(k[8], (64, 64), dtype=jnp.float32) / 8.0, 'mlp_b1': jnp.zeros((64,), dtype=jnp.float32), 'mlp_w2': jax.random.normal(k[9], (64, 4 * MUL), dtype=jnp.float32) / 8.0, 'mlp_b2': jnp.zeros((4 * MUL,), dtype=jnp.float32), 'W_out0': jax.random.normal(k[10], (2 * MUL, MUL), dtype=jnp.float32), 'W_out1': jax.random.normal(k[11], (2 * MUL, MUL), dtype=jnp.float32)}
        return inp
    _L1_gnn_all = _L1_gnn_setup()
    _L1_gnn_in = {k: v for k, v in _L1_gnn_all.items() if k in ('W_up0', 'W_up1', 'mlp_w0', 'mlp_b0', 'mlp_w1', 'mlp_b1', 'mlp_w2', 'mlp_b2', 'W_out0', 'W_out1')}
    del _L1_gnn_all

    def _L2_gnn_setup():
        import jax, jax.numpy as jnp
        import numpy as np
        N = 3125
        E = 20000
        D = 128

        def _weighted_mean_agg(ft, w, src, dst, n_nodes):
            m = ft[src] * w[:, None]
            msum = jax.ops.segment_sum(m, dst, num_segments=n_nodes)
            wsum = jax.ops.segment_sum(w, dst, num_segments=n_nodes)
            safe = jnp.where(wsum > 0, wsum, 1.0)
            return jnp.where((wsum > 0)[:, None], msum / safe[:, None], 0.0)
        key = jax.random.key(seed)
        ks = jax.random.split(key, 10)
        s = 1.0 / np.sqrt(D)
        feat = jax.random.normal(ks[0], (N, D), jnp.float32)
        w = jax.random.uniform(ks[1], (E,), jnp.float32)
        src = jax.random.randint(ks[2], (E,), 0, N, dtype=jnp.int32)
        dst = jax.random.randint(ks[3], (E,), 0, N, dtype=jnp.int32)
        W1 = jax.random.uniform(ks[4], (D, D), jnp.float32, -s, s)
        W2 = jax.random.uniform(ks[5], (D, D), jnp.float32, -s, s)
        sg = 1.0 / np.sqrt(D)
        w_ih = jax.random.uniform(ks[6], (3 * D, 2 * D), jnp.float32, -sg, sg)
        w_hh = jax.random.uniform(ks[7], (3 * D, D), jnp.float32, -sg, sg)
        b_ih = jax.random.uniform(ks[8], (3 * D,), jnp.float32, -sg, sg)
        b_hh = jax.random.uniform(ks[9], (3 * D,), jnp.float32, -sg, sg)
        return {'feat': feat, 'w': w, 'src': src, 'dst': dst, 'W1': W1, 'W2': W2, 'w_ih': w_ih, 'w_hh': w_hh, 'b_ih': b_ih, 'b_hh': b_hh}
    _L2_gnn_all = _L2_gnn_setup()
    _L2_gnn_in = {k: v for k, v in _L2_gnn_all.items() if k in ('W1', 'W2', 'w_ih', 'w_hh', 'b_ih', 'b_hh')}
    del _L2_gnn_all

    def _L3_gnn_setup():
        import jax, jax.numpy as jnp
        import numpy as np

        def gcn_norm(row, col, edge_weight, n):
            loop = jnp.arange(n, dtype=row.dtype)
            row2 = jnp.concatenate([row, loop])
            col2 = jnp.concatenate([col, loop])
            w2 = jnp.concatenate([edge_weight, jnp.ones((n,), edge_weight.dtype)])
            deg = jax.ops.segment_sum(w2, col2, num_segments=n)
            dis = jnp.where(deg > 0, jax.lax.rsqrt(deg), jnp.zeros((), deg.dtype))
            norm = dis[row2] * w2 * dis[col2]
            return (row2, col2, norm)

        def gcn_conv(x, row, col, norm, W, b, n):
            h = x @ W
            msg = norm[:, None] * h[row]
            out = jax.ops.segment_sum(msg, col, num_segments=n)
            return out + b
        key = jax.random.key(seed)
        k1, k2, k3, k4, k5 = jax.random.split(key, 5)
        N, E, F = (3125, 50000, 128)
        x = jax.random.normal(k1, (N, F), dtype=jnp.float32)
        edge_index = jax.random.randint(k2, (2, E), 0, N, dtype=jnp.int32)
        edge_weight = jax.random.uniform(k3, (E,), dtype=jnp.float32)
        s = 1.0 / np.sqrt(F)
        W1 = jax.random.uniform(k4, (F, F), dtype=jnp.float32, minval=-s, maxval=s)
        W2 = jax.random.uniform(k5, (F, F), dtype=jnp.float32, minval=-s, maxval=s)
        b1 = jnp.zeros((F,), jnp.float32)
        b2 = jnp.zeros((F,), jnp.float32)
        return {'x': x, 'edge_index': edge_index, 'edge_weight': edge_weight, 'W1': W1, 'b1': b1, 'W2': W2, 'b2': b2}
    _L3_gnn_all = _L3_gnn_setup()
    _L3_gnn_in = {k: v for k, v in _L3_gnn_all.items() if k in ('W1', 'b1', 'W2', 'b2')}
    del _L3_gnn_all
    return {'x': x, 'src': src, 'dst': dst, 'edge_attr_3': edge_attr_3, 'edge_weight': edge_weight, 'L0_gnn_W': _L0_gnn_in['W'], 'L0_gnn_b': _L0_gnn_in['b'], 'L1_gnn_W_up0': _L1_gnn_in['W_up0'], 'L1_gnn_W_up1': _L1_gnn_in['W_up1'], 'L1_gnn_mlp_w0': _L1_gnn_in['mlp_w0'], 'L1_gnn_mlp_b0': _L1_gnn_in['mlp_b0'], 'L1_gnn_mlp_w1': _L1_gnn_in['mlp_w1'], 'L1_gnn_mlp_b1': _L1_gnn_in['mlp_b1'], 'L1_gnn_mlp_w2': _L1_gnn_in['mlp_w2'], 'L1_gnn_mlp_b2': _L1_gnn_in['mlp_b2'], 'L1_gnn_W_out0': _L1_gnn_in['W_out0'], 'L1_gnn_W_out1': _L1_gnn_in['W_out1'], 'L2_gnn_W1': _L2_gnn_in['W1'], 'L2_gnn_W2': _L2_gnn_in['W2'], 'L2_gnn_w_ih': _L2_gnn_in['w_ih'], 'L2_gnn_w_hh': _L2_gnn_in['w_hh'], 'L2_gnn_b_ih': _L2_gnn_in['b_ih'], 'L2_gnn_b_hh': _L2_gnn_in['b_hh'], 'L3_gnn_W1': _L3_gnn_in['W1'], 'L3_gnn_b1': _L3_gnn_in['b1'], 'L3_gnn_W2': _L3_gnn_in['W2'], 'L3_gnn_b2': _L3_gnn_in['b2']}

def reference(x, src, dst, edge_attr_3, edge_weight, L0_gnn_W, L0_gnn_b, L1_gnn_W_up0, L1_gnn_W_up1, L1_gnn_mlp_w0, L1_gnn_mlp_b0, L1_gnn_mlp_w1, L1_gnn_mlp_b1, L1_gnn_mlp_w2, L1_gnn_mlp_b2, L1_gnn_W_out0, L1_gnn_W_out1, L2_gnn_W1, L2_gnn_W2, L2_gnn_w_ih, L2_gnn_w_hh, L2_gnn_b_ih, L2_gnn_b_hh, L3_gnn_W1, L3_gnn_b1, L3_gnn_W2, L3_gnn_b2):
    import jax
    import jax.numpy as jnp

    def _L0_gnn_ref(h, src, dst, W, b):
        import jax, jax.numpy as jnp
        import numpy as np
        N_NODES = 3125
        N_EDGES = 50000
        D_IN = 128
        D_OUT = 128
        n = h.shape[0]
        msg = h[src]
        summed = jax.ops.segment_sum(msg, dst, num_segments=n)
        deg = jax.ops.segment_sum(jnp.ones((src.shape[0],), h.dtype), dst, num_segments=n)
        h_N = summed / jnp.maximum(deg, 1.0)[:, None]
        h_total = jnp.concatenate([h, h_N], axis=1)
        return h_total @ W.T + b

    def _L1_gnn_ref(node_feats, edge_vec, edge_length, senders, receivers, num_nodes, W_up0, W_up1, mlp_w0, mlp_b0, mlp_w1, mlp_b1, mlp_w2, mlp_b2, W_out0, W_out1):
        import jax, jax.numpy as jnp
        import numpy as np
        N = 50000
        E = 25000
        MUL = 32
        NB = 8
        R_MAX = 1.0
        AVG = 16.0
        SQ3 = 3.0 ** 0.5

        def _radial_embedding(r):
            x = jnp.clip(r / R_MAX, 0.0, 1.0)
            centers = jnp.arange(NB, dtype=jnp.float32) / (NB - 1)
            sigma = 1.0 / (NB - 1)
            emb = jnp.exp(-0.5 * ((x[:, None] - centers[None, :]) / sigma) ** 2)
            emb = emb * NB ** 0.5 * (r <= R_MAX).astype(jnp.float32)[:, None]
            return emb
        f32 = jnp.float32
        rhat = edge_vec / (jnp.linalg.norm(edge_vec, axis=-1, keepdims=True) + 1e-12)
        Y1 = SQ3 * rhat
        emb = _radial_embedding(edge_length)
        h = jax.nn.silu(emb @ mlp_w0 + mlp_b0)
        h = jax.nn.silu(h @ mlp_w1 + mlp_b1)
        w = (h @ mlp_w2 + mlp_b2).reshape(-1, 4, MUL)
        s = node_feats[:, :MUL]
        v = node_feats[:, MUL:].reshape(-1, MUL, 3)
        xs = s @ W_up0 / f32(MUL) ** 0.5
        xv = jnp.einsum('nmc,mk->nkc', v, W_up1) / f32(MUL) ** 0.5
        ss = xs[senders]
        vv = xv[senders]
        m0 = w[:, 0] * ss
        m1 = w[:, 1][:, :, None] * ss[:, :, None] * Y1[:, None, :]
        m2 = w[:, 2][:, :, None] * vv
        m3 = w[:, 3] * (jnp.einsum('emc,ec->em', vv, Y1) / SQ3)
        mid_s = jnp.concatenate([m0, m3], axis=1)
        mid_v = jnp.concatenate([m1, m2], axis=1)
        msg_s = jax.ops.segment_sum(mid_s, receivers, num_segments=num_nodes)
        msg_v = jax.ops.segment_sum(mid_v, receivers, num_segments=num_nodes)
        out_s = msg_s @ W_out0 / f32(2 * MUL) ** 0.5
        out_v = jnp.einsum('nmc,mk->nkc', msg_v, W_out1) / f32(2 * MUL) ** 0.5
        out = jnp.concatenate([out_s, out_v.reshape(-1, 3 * MUL)], axis=1)
        return out / max(AVG, 1e-08)

    def _L2_gnn_ref(feat, w, src, dst, W1, W2, w_ih, w_hh, b_ih, b_hh):
        import jax, jax.numpy as jnp
        import numpy as np
        N = 3125
        E = 20000
        D = 128

        def _weighted_mean_agg(ft, w, src, dst, n_nodes):
            m = ft[src] * w[:, None]
            msum = jax.ops.segment_sum(m, dst, num_segments=n_nodes)
            wsum = jax.ops.segment_sum(w, dst, num_segments=n_nodes)
            safe = jnp.where(wsum > 0, wsum, 1.0)
            return jnp.where((wsum > 0)[:, None], msum / safe[:, None], 0.0)
        n = feat.shape[0]
        neigh1 = _weighted_mean_agg(feat, w, src, dst, n)
        neigh2 = _weighted_mean_agg(feat, w, dst, src, n)
        hn = jnp.concatenate([neigh1 @ W1.T, neigh2 @ W2.T], axis=1)
        gi = hn @ w_ih.T + b_ih
        gh = feat @ w_hh.T + b_hh
        i_r, i_z, i_n = jnp.split(gi, 3, axis=1)
        h_r, h_z, h_n = jnp.split(gh, 3, axis=1)
        r = jax.nn.sigmoid(i_r + h_r)
        z = jax.nn.sigmoid(i_z + h_z)
        nn_ = jnp.tanh(i_n + r * h_n)
        return nn_ + z * (feat - nn_)

    def _L3_gnn_ref(x, edge_index, edge_weight, W1, b1, W2, b2):
        import jax, jax.numpy as jnp
        import numpy as np

        def gcn_norm(row, col, edge_weight, n):
            loop = jnp.arange(n, dtype=row.dtype)
            row2 = jnp.concatenate([row, loop])
            col2 = jnp.concatenate([col, loop])
            w2 = jnp.concatenate([edge_weight, jnp.ones((n,), edge_weight.dtype)])
            deg = jax.ops.segment_sum(w2, col2, num_segments=n)
            dis = jnp.where(deg > 0, jax.lax.rsqrt(deg), jnp.zeros((), deg.dtype))
            norm = dis[row2] * w2 * dis[col2]
            return (row2, col2, norm)

        def gcn_conv(x, row, col, norm, W, b, n):
            h = x @ W
            msg = norm[:, None] * h[row]
            out = jax.ops.segment_sum(msg, col, num_segments=n)
            return out + b
        n = x.shape[0]
        row, col = (edge_index[0], edge_index[1])
        row2, col2, norm = gcn_norm(row, col, edge_weight, n)
        h = gcn_conv(x, row2, col2, norm, W1, b1, n)
        h = jax.nn.relu(h)
        out = gcn_conv(h, row2, col2, norm, W2, b2, n)
        return out
    edge_index = jnp.stack([src, dst])
    h = jnp.maximum(_layernorm(x, axis=-1), 0.0)
    x = x + _L0_gnn_ref(h, src, dst, L0_gnn_W, L0_gnn_b)
    h = jnp.maximum(_layernorm(x, axis=-1), 0.0)
    x = x + _L1_gnn_ref(h, edge_attr_3, edge_weight, src, dst, 50000, L1_gnn_W_up0, L1_gnn_W_up1, L1_gnn_mlp_w0, L1_gnn_mlp_b0, L1_gnn_mlp_w1, L1_gnn_mlp_b1, L1_gnn_mlp_w2, L1_gnn_mlp_b2, L1_gnn_W_out0, L1_gnn_W_out1)
    h = jnp.maximum(_layernorm(x, axis=-1), 0.0)
    x = x + _L2_gnn_ref(h, edge_weight, src, dst, L2_gnn_W1, L2_gnn_W2, L2_gnn_w_ih, L2_gnn_w_hh, L2_gnn_b_ih, L2_gnn_b_hh)
    h = jnp.maximum(_layernorm(x, axis=-1), 0.0)
    x = x + _L3_gnn_ref(h, edge_index, edge_weight, L3_gnn_W1, L3_gnn_b1, L3_gnn_W2, L3_gnn_b2)
    return x

_drawn_inputs = setup_inputs


def setup_inputs(seed=0):
    import zlib

    import numpy as np

    out = dict(_drawn_inputs(seed))
    spreads = {'L0_gnn_b': (0.0, 0.1),
     'L1_gnn_mlp_b0': (0.0, 0.8),
     'L1_gnn_mlp_b1': (0.0, 0.8),
     'L1_gnn_mlp_b2': (0.0, 0.8),
     'L3_gnn_b1': (0.0, 2.0),
     'L3_gnn_b2': (0.0, 2.0)}
    factors = {'edge_attr_3': 5.887,
     'L1_gnn_W_up0': 5.408,
     'L1_gnn_W_up1': 4.412,
     'L1_gnn_mlp_w0': 4.11,
     'L1_gnn_mlp_w1': 3.691,
     'L1_gnn_mlp_w2': 3.466,
     'L1_gnn_W_out0': 7.39,
     'L1_gnn_W_out1': 4.242,
     'L2_gnn_b_ih': 23.176,
     'L2_gnn_b_hh': 40.864,
     'L2_gnn_W1': 33.797,
     'L2_gnn_W2': 8.0,
     'L2_gnn_w_ih': 8.0,
     'L2_gnn_w_hh': 8.0,
     'L3_gnn_W1': 8.0,
     'L3_gnn_W2': 8.0}
    for name, (base, spread) in spreads.items():
        noise = np.random.default_rng([zlib.crc32(name.encode()), seed]).standard_normal(out[name].shape)
        drawn = base * np.exp(spread * noise) if base else spread * noise
        out[name] = jnp.asarray(drawn.astype(out[name].dtype))
    for name, factor in factors.items():
        out[name] = (out[name] * factor).astype(out[name].dtype)
    return out
```

```python
import concourse.bass as bass
from concourse import mybir
from contextlib import ExitStack

P = 128
D = 128
GB = 4
RING = 2 * GB
MUL = 32
NBASIS = 8
HID = 64
LN_EPS = 1e-5
SQ3 = 3.0 ** 0.5
OUT_SCALE = (2 * MUL) ** -0.5 / 16.0

f32 = mybir.dt.float32
i32 = mybir.dt.int32
ALU = mybir.AluOpType
ACT = mybir.ActivationFunctionType
AX = mybir.AxisListType


def blocks_of(table, first, count, width=D):
    return table[bass.ds(first, count * P), 0:width].rearrange("(j p) f -> p j f", p=P)


def row_of(vector, first, count, lanes):
    return vector.rearrange("(a e) -> a e", a=1)[:, bass.ds(first, count)].to_broadcast((lanes, count))


class Memory:

    def __init__(self, nc, ctx):
        self.nc, self.ctx, self.sems = nc, ctx, []
        ctx.callback(self.close)

    def close(self):
        if self.sems:
            self.nc.clear_and_free_semaphores(self.sems)
            self.nc.all_engine_barrier()

    def sb(self, name, shape, dt=f32):
        return self.ctx.enter_context(self.nc.sbuf_tensor(name, shape, dt))

    def ps(self, name, shape):
        return self.ctx.enter_context(self.nc.psum_tensor(name, shape, f32))

    def sem(self, name):
        self.sems.append(self.nc.alloc_semaphore(name))
        return self.sems[-1]


def setup_pass(nc, A, S, T, NT, NODES):
    TB = NT // 4
    with ExitStack() as ctx:
        m = Memory(nc, ctx)
        lane_i = m.sb("lane_i", [P, P], i32)
        part_i = m.sb("part_i", [P, 1], i32)
        lane = m.sb("lane", [P, P])
        rows_i = m.sb("rows_i", [TB, 2, 4, P], i32)
        rows = m.sb("rows", [TB, 3, 4, P])
        vec_rows = m.sb("vec_rows", [TB, 4, 3 * P])
        square = m.sb("square", [P, NT, 3])
        norm = m.sb("norm", [P, NT])
        zeros = m.sb("zeros", [P, 8 * 132])
        w0 = m.sb("w0_rows", [P, 2 * D])
        wih = m.sb("wih_rows", [P, 3, 2 * D])
        wihT = m.sb("wihT", [P, 2, 3 * D])
        whh = m.sb("whh_rows", [P, 3, D])
        wl2 = m.sb("wl2", [P, 2, D])
        wup0 = m.sb("wup0", [MUL, MUL])
        wout0 = m.sb("wout0", [2 * MUL, MUL])
        wout1 = m.sb("wout1", [P, 2, MUL])
        bank = [m.ps(f"setup_bank{k}", [P, 512]) for k in range(8)]
        s_iota = m.sem("su_iota")
        s_cast = m.sem("su_iota_cast")
        s_zero = m.sem("su_zeros_set")
        s_zst = m.sem("su_zeros_stored")
        s_const = m.sem("su_constants_set")
        s_in = m.sem("su_loaded")
        s_rows = m.sem("su_rows_are_float")
        s_tr = m.sem("su_transposed")
        s_ev = m.sem("su_evacuated")
        s_sq = m.sem("su_squared")
        s_n2 = m.sem("su_norm2_ready")
        s_root = m.sem("su_norm_ready")
        s_inv = m.sem("su_norm_inverted")
        s_wT = m.sem("su_wihT_ready")
        s_pr = m.sem("su_gru_products")

        loads = []

        def load(dst, src):
            loads.append((dst, src))

        for k, name in enumerate(("src", "dst")):
            load(rows_i[:, k], A[name].rearrange("(c t p) -> t c p", c=4, p=P))
        load(rows[:, 2], A["edge_weight"].rearrange("(c t p) -> t c p", c=4, p=P))
        load(vec_rows[:, :, :], A["edge_attr_3"].rearrange("(c t p) k -> t c (p k)", c=4, p=P))
        load(w0[:, :], A["L0_gnn_W"])
        load(wih[:, :, :], A["L2_gnn_w_ih"].rearrange("(k p) f -> p k f", p=P))
        load(whh[:, :, :], A["L2_gnn_w_hh"].rearrange("(k p) f -> p k f", p=P))
        load(wl2[:, 0], A["L2_gnn_W1"])
        load(wl2[:, 1], A["L2_gnn_W2"])
        load(S["w31"][:, :], A["L3_gnn_W1"])
        load(S["w32"][:, :], A["L3_gnn_W2"])
        load(wup0[:, :], A["L1_gnn_W_up0"])
        for c in range(3):
            load(S["wup"][MUL + c:P:3, 32 + 32 * c:64 + 32 * c], A["L1_gnn_W_up1"])
        load(wout0[:, :], A["L1_gnn_W_out0"])
        for c in range(2):
            load(wout1[64 + 32 * c:96 + 32 * c, 0], A["L1_gnn_W_out1"][0:MUL, :])
        load(wout1[0:32, 1], A["L1_gnn_W_out1"][0:MUL, :])
        for c in range(3):
            load(wout1[32 + 32 * c:64 + 32 * c, 1], A["L1_gnn_W_out1"][MUL:2 * MUL, :])
        load(S["mw0"][:, :], A["L1_gnn_mlp_w0"])
        load(S["mw1"][:, :], A["L1_gnn_mlp_w1"])
        load(S["mw2"][0:HID, :], A["L1_gnn_mlp_w2"])
        load(S["mw2"][HID:HID + 1, :], A["L1_gnn_mlp_b2"].rearrange("(a f) -> a f", a=1))
        load(S["mb0"][:, 0:1], A["L1_gnn_mlp_b0"].rearrange("(f a) -> f a", a=1))
        load(S["mb1"][:, 0:1], A["L1_gnn_mlp_b1"].rearrange("(f a) -> f a", a=1))
        load(S["b0"][:, :], row_of(A["L0_gnn_b"], 0, D, P))
        load(S["b31"][:, :], row_of(A["L3_gnn_b1"], 0, D, P))
        load(S["b32"][:, :], row_of(A["L3_gnn_b2"], 0, D, P))
        load(S["bih"][:, :], row_of(A["L2_gnn_b_ih"], 0, 3 * D, P))
        load(S["bhh"][:, :], row_of(A["L2_gnn_b_hh"], 0, 3 * D, P))

        with nc.Block() as block:
            @block.sync
            def _(sp):
                sp.wait_ge(s_const, 1)
                for dst, src in loads:
                    sp.dma_start(dst, src).then_inc(s_in, 16)
                sp.wait_ge(s_zero, 1)
                stored, per = 0, 8
                for name in ("acc0", "acc2", "acc2b"):
                    t = T[name]
                    whole = t.shape[0] // P // per
                    rest = t.shape[0] // P - whole * per
                    width = t.shape[1]
                    with sp.Fori(0, whole) as i:
                        sp.dma_start(t[bass.ds(i * (per * P), per * P), :].rearrange("(p j) f -> p (j f)", p=P),
                                     zeros[:, 0:per * width]).then_inc(s_zst, 16)
                    stored += 16 * whole
                    if rest:
                        sp.dma_start(t[whole * per * P:t.shape[0], :].rearrange("(p j) f -> p (j f)", p=P),
                                     zeros[:, 0:rest * width]).then_inc(s_zst, 16)
                        stored += 16
                sp.wait_ge(s_zst, stored)

            @block.gpsimd
            def _(pool):
                nc.gpsimd.iota(lane_i[:, :], [[1, P]], 0, 0)
                nc.gpsimd.iota(part_i[:, :], [[0, 1]], 0, 1).then_inc(s_iota, 1)
                pool.wait_ge(s_iota, 1)
                nc.gpsimd.tensor_copy(lane[:, :], lane_i[:, :])
                nc.gpsimd.tensor_copy(S["part"][:, :], part_i[:, :]).then_inc(s_cast, 1)
                nc.gpsimd.memset(zeros[:, :], 0.0).then_inc(s_zero, 1)

            @block.scalar
            def _(act):
                act.wait_ge(s_n2, 1)
                nc.scalar.activation(norm[:, :], norm[:, :], ACT.Sqrt).then_inc(s_root, 1)

            @block.tensor
            def _(pe):
                pe.wait_ge(s_rows, 1)
                for k in range(3):
                    for c in range(4):
                        last = nc.tensor.transpose(bank[k][:, c * TB:(c + 1) * TB], rows[:, k, c, :],
                                                   S["ident"][0:TB, 0:TB])
                last.then_inc(s_tr, 1)
                for k in range(3):
                    for c in range(4):
                        last = nc.tensor.transpose(
                            bank[3 + k][:, c * TB:(c + 1) * TB],
                            vec_rows[:, c, :].rearrange("t (p k) -> t k p", k=3)[:, k, :], S["ident"][0:TB, 0:TB])
                last.then_inc(s_tr, 1)
                for h in range(2):
                    last = nc.tensor.transpose(bank[6][:, h * D:(h + 1) * D], w0[:, h * D:(h + 1) * D], S["ident"][:, :])
                for k in range(3):
                    last = nc.tensor.transpose(bank[7][:, k * D:(k + 1) * D], whh[:, k, :], S["ident"][:, :])
                last.then_inc(s_tr, 1)
                pe.wait_ge(s_ev, 1)
                for h in range(2):
                    for k in range(3):
                        last = nc.tensor.transpose(bank[h][:, k * D:(k + 1) * D], wih[:, k, h * D:(h + 1) * D],
                                                   S["ident"][:, :])
                last.then_inc(s_tr, 1)
                pe.wait_ge(s_wT, 1)
                pe.wait_ge(s_ev, 3)
                for h in range(2):
                    last = nc.tensor.matmul(bank[6 + h][:, 0:3 * D], wl2[:, h, :], wihT[:, h, :], start=True, stop=True)
                last.then_inc(s_pr, 1)

            @block.vector
            def _(dve):
                nc.vector.memset(S["wup"][:, :], 0.0)
                nc.vector.memset(S["wout"][:, :, :], 0.0)
                nc.vector.memset(S["hid2"][:, :, :], 1.0)
                nc.vector.memset(S["onew"][:, :, :], 1.0)
                nc.vector.memset(S["eps"][:, :], LN_EPS)
                dve.wait_ge(s_cast, 1)
                nc.vector.tensor_scalar(S["ident"][:, :], lane[:, :], S["part"][:, 0:1], None, ALU.is_equal)
                nc.vector.tensor_scalar(S["earlier"][:, :], lane[:, :], S["part"][:, 0:1], None, ALU.is_lt)
                nc.vector.tensor_scalar(S["spare"][:, :], S["part"][:, :], float(NODES), None, ALU.add)
                nc.vector.tensor_scalar(S["ncen"][:, :], S["part"][0:NBASIS, :], -1.0, None,
                                        ALU.mult).then_inc(s_const, 1)
                dve.wait_ge(s_in, 16 * len(loads))
                nc.vector.tensor_copy(rows[:, 0:2], rows_i[:, :]).then_inc(s_rows, 1)
                nc.vector.tensor_scalar(S["mw1"][:, :], S["mw1"][:, :], 0.5, None, ALU.mult)
                nc.vector.tensor_scalar(S["mw2"][0:HID, :], S["mw2"][0:HID, :], 0.5, None, ALU.mult)
                nc.vector.tensor_scalar(S["mb0"][:, 1:2], S["mb0"][:, 0:1], 0.5, None, ALU.mult)
                nc.vector.tensor_scalar(S["mb1"][:, 1:2], S["mb1"][:, 0:1], 0.5, None, ALU.mult)
                nc.vector.tensor_scalar(S["wup"][0:MUL, 0:MUL], wup0[:, :], MUL ** -0.5, None, ALU.mult)
                for lo in (32, 64, 96):
                    nc.vector.tensor_scalar(S["wup"][lo:lo + 32, 32:P], S["wup"][lo:lo + 32, 32:P], MUL ** -0.5,
                                            None, ALU.mult)
                nc.vector.tensor_scalar(S["wout"][0:64, 0, 0:MUL], wout0[:, :], OUT_SCALE, None, ALU.mult)
                for half, lo, c in ((0, 64, 0), (0, 96, 1), (1, 0, 2), (1, 32, 0), (1, 64, 1), (1, 96, 2)):
                    nc.vector.tensor_scalar(S["wout"][lo:lo + 32, half, 32 + c:D:3], wout1[lo:lo + 32, half, :],
                                            OUT_SCALE, None, ALU.mult)
                dve.wait_ge(s_tr, 1)
                nc.vector.tensor_copy(S["srcf"][:, :], bank[0][:, 0:NT])
                nc.vector.tensor_copy(S["srci"][:, :], bank[0][:, 0:NT])
                nc.vector.tensor_copy(S["dstf"][:, :], bank[1][:, 0:NT])
                nc.vector.tensor_copy(S["dsti"][:, :], bank[1][:, 0:NT])
                nc.vector.tensor_copy(S["onew"][:, :, 1], bank[2][:, 0:NT])
                nc.vector.tensor_copy(S["w"][:, :], bank[2][:, 0:NT]).then_inc(s_ev, 1)
                dve.wait_ge(s_tr, 2)
                for k in range(3):
                    last = nc.vector.tensor_copy(S["rhat"][:, :, k], bank[3 + k][:, 0:NT])
                last.then_inc(s_ev, 1)
                dve.wait_ge(s_ev, 2)
                nc.vector.tensor_tensor(square[:, :, :], S["rhat"][:, :, :], S["rhat"][:, :, :],
                                        ALU.mult).then_inc(s_sq, 1)
                dve.wait_ge(s_sq, 1)
                nc.vector.tensor_reduce(norm[:, :], square[:, :, :], AX.X, ALU.add).then_inc(s_n2, 1)
                dve.wait_ge(s_tr, 3)
                nc.vector.tensor_copy(S["w0s"][:, :], bank[6][:, 0:D])
                nc.vector.tensor_copy(S["w0n"][:, :], bank[6][:, D:2 * D])
                nc.vector.tensor_copy(S["whh"][:, :], bank[7][:, 0:3 * D]).then_inc(s_ev, 1)
                dve.wait_ge(s_tr, 4)
                for h in range(2):
                    last = nc.vector.tensor_copy(wihT[:, h, :], bank[h][:, 0:3 * D])
                last.then_inc(s_wT, 1)
                dve.wait_ge(s_pr, 1)
                for h in range(2):
                    nc.vector.tensor_copy(S["wih"][:, h, :], bank[6 + h][:, 0:3 * D])
                dve.wait_ge(s_root, 1)
                nc.vector.tensor_scalar(norm[:, :], norm[:, :], 1e-12, None, ALU.add).then_inc(s_inv, 1)
                dve.wait_ge(s_inv, 1)
                nc.vector.reciprocal(norm[:, :], norm[:, :]).then_inc(s_inv, 1)
                dve.wait_ge(s_inv, 2)
                nc.vector.tensor_tensor(S["rhat"][:, :, :], S["rhat"][:, :, :],
                                        norm[:, :].unsqueeze(2).to_broadcast((P, NT, 3)), ALU.mult).then_inc(s_inv, 1)
                dve.wait_ge(s_inv, 3)
                nc.vector.tensor_scalar(S["y1c"][:, :, :], S["rhat"][:, :, :], SQ3, None, ALU.mult)


def unique_pass(nc, A, S, NT):
    STEPS = NT // RING
    with ExitStack() as ctx:
        m = Memory(nc, ctx)
        row = [[m.sb(f"un_row{k}{h}", [P, GB * P], i32) for h in range(2)] for k in range(2)]
        junk = m.sb("un_junk", [P, 2, 2, GB, P])
        dup = [m.sb(f"un_dup{k}", [P, NT]) for k in range(2)]
        away = [m.sb(f"un_away{k}", [P, NT]) for k in range(2)]
        s_row = [m.sem(f"un_rows_loaded{h}") for h in range(2)]
        s_cnt = m.sem("un_tiles_counted")
        s_fin = m.sem("un_list_step")
        with nc.Block() as block:
            @block.sync
            def _(sp):
                def half(i, h, first):
                    if not first:
                        sp.wait_ge(s_cnt, 2 * (i * 2 + h - 1))
                    for k, name in enumerate(("src", "dst")):
                        sp.dma_start(row[k][h][:, :], row_of(A[name], i * (RING * P) + h * (GB * P), GB * P, P)
                                     ).then_inc(s_row[h], 16)

                for h in range(2):
                    half(0, h, True)
                with sp.Fori(1, STEPS) as i:
                    for h in range(2):
                        half(i, h, False)

            @block.vector
            def _(dve):
                def half(i, h, first):
                    dve.wait_ge(s_row[h], i * 32 + 32)
                    if not first:
                        dve.wait_ge(s_cnt, 2 * (i * 2 + h - 1))
                    for k, col in enumerate((S["srcf"], S["dstf"])):
                        for j in range(GB):
                            t = i * RING + h * GB + j
                            last = nc.vector.scalar_tensor_tensor(
                                out=junk[:, h, k, j, :], in0=row[k][h][:, j * P:(j + 1) * P],
                                scalar=col[:, bass.ds(t, 1)], in1=S["earlier"][:, :],
                                op0=ALU.is_equal, op1=ALU.mult, accum_out=dup[k][:, bass.ds(t, 1)])
                        last.then_inc(s_cnt, 1)

                for h in range(2):
                    half(0, h, True)
                with dve.Fori(1, STEPS) as i:
                    for h in range(2):
                        half(i, h, False)
                dve.wait_ge(s_cnt, 4 * STEPS)
                for k, (col, out) in enumerate(((S["srcf"], S["srcu"]), (S["dstf"], S["dstu"]))):
                    nc.vector.tensor_scalar(away[k][:, :], col[:, :], S["spare"][:, 0:1], -1.0,
                                            ALU.subtract, ALU.mult).then_inc(s_fin, 1)
                    dve.wait_ge(s_fin, 3 * k + 1)
                    nc.vector.scalar_tensor_tensor(out=away[k][:, :], in0=dup[k][:, :], scalar=1.0,
                                                   in1=away[k][:, :], op0=ALU.min, op1=ALU.mult).then_inc(s_fin, 1)
                    dve.wait_ge(s_fin, 3 * k + 2)
                    nc.vector.tensor_tensor(out[:, :], away[k][:, :], col[:, :], ALU.add).then_inc(s_fin, 1)


def edge_pass(nc, A, S, T, NT, X, table, acc, gather, target, weighted, extra):
    STEPS = NT // RING
    width = D + {"": 0, "deg": 2, "w": 1}[extra]
    gidx = S[gather + "i"]
    sidx = S[target + "u"]
    col = S[target + "f"]
    ring, comb, eq, row, bank = X["ring"], X["comb"], X["eq"], X["row"], X["bank"]
    gslot, sslot = X["gslot"], X["sslot"]
    s_gath, s_row, s_eq = X["s_gath"], X["s_row"], X["s_eq"]
    s_mm, s_ev, s_scat, s_gidx, s_sidx = X["s_mm"], X["s_ev"], X["s_scat"], X["s_gidx"], X["s_sidx"]
    s_go = X["s_go"]
    table, acc, names = T[table], T[acc], A[target]

    with nc.Block() as block:
        @block.sync
        def _(sp):
            def half(i, h, first):
                if not first:
                    sp.wait_ge(s_eq, i * RING + (h - 1) * GB)
                sp.dma_start(row[h][:, :], row_of(names, i * (RING * P) + h * (GB * P), GB * P, P)
                             ).then_inc(s_row[h], 16)

            for h in range(2):
                half(0, h, True)
            with sp.Fori(1, STEPS) as i:
                for h in range(2):
                    half(i, h, False)

        @block.gpsimd
        def _(pool):
            def fresh(t, half, slots, column, done, i):
                nc.gpsimd.tensor_copy(slots[:, half * GB:(half + 1) * GB], column[:, bass.ds(t, GB)]).then_inc(done, 1)

            def gather(i, j, first):
                t = i * RING + j
                if j % GB == 0:
                    if not first:
                        pool.wait_ge(s_mm, t - GB)
                    fresh(t, j // GB, gslot, gidx, s_gidx, i)
                    pool.wait_ge(s_gidx, i * 2 + j // GB + 1)
                if not first:
                    pool.wait_ge(s_mm, t - RING + 1)
                pool.sem_inc(s_go, 1)
                pool.indirect_dma_start(ring[:, j, :], None, table[:, :],
                                        bass.IndirectOffsetOnAxis(ap=gslot[:, j:j + 1], axis=0)
                                        ).then_inc(s_gath[j], 16)

            def scatter(i, j, first, refill=True):
                t, slot = i * RING + j - GB, (j + GB) % RING
                started = not (first and j < GB)
                if started and not (first and j == GB):
                    pool.wait_ge(s_scat, t * 16)
                if j % GB == 0 and refill:
                    fresh(t + GB, j // GB, sslot, sidx, s_sidx, i)
                if started:
                    if j % GB == 0:
                        pool.wait_ge(s_sidx, i * 2 + j // GB)
                    pool.wait_ge(s_ev, t + 1)
                    pool.sem_inc(s_go, 1)
                    pool.indirect_dma_start(acc[:, :], bass.IndirectOffsetOnAxis(ap=sslot[:, slot:slot + 1], axis=0),
                                            comb[:, slot, 0:width], None, compute_op=ALU.add).then_inc(s_scat, 16)

            def step(i, first):
                for j in range(RING):
                    gather(i, j, first)
                    scatter(i, j, first)

            step(0, True)
            with pool.Fori(1, STEPS) as i:
                step(i, False)
            for j in range(GB):
                scatter(STEPS, j, False, refill=False)
            pool.wait_ge(s_scat, NT * 16)

        @block.vector
        def _(dve):
            def step(i, first):
                for j in range(RING):
                    t = i * RING + j
                    if j % GB == 0:
                        dve.wait_ge(s_row[j // GB], i * 16 + 16)
                    if not (first and j < GB):
                        dve.wait_ge(s_mm, t - GB + 1)
                    weight = (S["w"][:, bass.ds(t, 1)], ALU.mult) if weighted else (None,)
                    nc.vector.tensor_scalar(eq[:, j % GB, :], row[j // GB][:, (j % GB) * P:(j % GB + 1) * P],
                                            col[:, bass.ds(t, 1)], weight[0], ALU.is_equal,
                                            *weight[1:]).then_inc(s_eq, 1)

            step(0, True)
            with dve.Fori(1, STEPS) as i:
                step(i, False)

        @block.tensor
        def _(pe):
            def step(i, first):
                for j in range(RING):
                    t = i * RING + j
                    pe.wait_ge(s_gath[j], i * 16 + 16)
                    pe.wait_ge(s_eq, t + 1)
                    if not (first and j < GB):
                        pe.wait_ge(s_ev, t - GB + 1)
                    last = nc.tensor.matmul(bank[j % GB][:, 0:D], eq[:, j % GB, :], ring[:, j, :],
                                            start=True, stop=True)
                    if extra == "deg":
                        last = nc.tensor.matmul(bank[j % GB][:, D:D + 2], eq[:, j % GB, :],
                                                S["onew"][:, bass.ds(t, 1), :], start=True, stop=True)
                    if extra == "w":
                        last = nc.tensor.matmul(bank[j % GB][:, D:D + 1], eq[:, j % GB, :],
                                                S["onew"][:, 0, 0:1], start=True, stop=True)
                    last.then_inc(s_mm, 1)

            step(0, True)
            with pe.Fori(1, STEPS) as i:
                step(i, False)

        @block.scalar
        def _(act):
            def step(i, first):
                for j in range(RING):
                    t = i * RING + j
                    act.wait_ge(s_mm, t + 1)
                    if not first:
                        act.wait_ge(s_scat, (t - RING + 1) * 16)
                    nc.scalar.copy(comb[:, j, 0:width], bank[j % GB][:, 0:width]).then_inc(s_ev, 1)

            step(0, True)
            with act.Fori(1, STEPS) as i:
                step(i, False)


def node_pass(nc, S, T, NG, kind):
    has_ln = kind in ("in", "l0", "l1", "l2")
    has_mm = kind in ("in", "l0", "l2", "l3a")
    has_x = kind in ("in", "l0", "l3a", "l3b")
    cols = 2 * D if kind == "in" else D
    ins = {"in": [("x", D)], "l0": [("own", D), ("acc0", D + 2)], "l1": [("acc1", D)], "l2": [("x3", D)],
           "l3a": [("acc3", D)], "l3b": [("acc4", D), ("x3", D)]}[kind]
    weight = {"in": None, "l0": S["wup"], "l1": None, "l2": S["w31"], "l3a": S["w32"], "l3b": None}[kind]
    with ExitStack() as ctx:
        m = Memory(nc, ctx)
        src = [[m.sb(f"n_{kind}_{name}{u}", [P, GB, w]) for u in range(2)] for name, w in ins]
        xn = [m.sb(f"n_{kind}_x_new{u}", [P, GB, D]) for u in range(2)]
        h = [m.sb(f"n_{kind}_h{u}", [P, GB, D]) for u in range(2)]
        hT = [m.sb(f"n_{kind}_hT{u}", [P, GB, D]) for u in range(2)]
        y = [m.sb(f"n_{kind}_y{u}", [P, GB, cols]) for u in range(2)]
        plain = xn if kind == "l0" else src[0]
        small = [m.sb(f"n_{kind}_small{u}", [P, GB, 16]) for u in range(2)]
        psT = [m.ps(f"n_{kind}_psT{u}", [P, GB, D]) for u in range(2)]
        psY = [m.ps(f"n_{kind}_psY{u}", [P, GB, cols]) for u in range(2)]
        s_ld = [m.sem(f"n_{kind}_loaded{u}") for u in range(2)]
        s_x = m.sem(f"n_{kind}_x_ready")
        s_deg = m.sem(f"n_{kind}_degree_step")
        s_bn = m.sem(f"n_{kind}_stats_step")
        s_var = m.sem(f"n_{kind}_variance_ready")
        s_std = m.sem(f"n_{kind}_std_ready")
        s_rs = m.sem(f"n_{kind}_rstd_ready")
        s_nm = m.sem(f"n_{kind}_shift_ready")
        s_h = m.sem(f"n_{kind}_h_ready")
        s_T = m.sem(f"n_{kind}_transposed")
        s_hT = m.sem(f"n_{kind}_hT_ready")
        s_mm = m.sem(f"n_{kind}_product_ready")
        s_y = m.sem(f"n_{kind}_y_ready")
        s_st = [m.sem(f"n_{kind}_stored{u}") for u in range(2)]
        stores = {"in": [(y, 0, "y0"), (y, D, "own")], "l0": [(xn, 0, "acc1"), (y, 0, "y1")],
                  "l1": [(h, 0, "h2")], "l2": [(y, 0, "y3"), (y, 0, "acc3")], "l3a": [(y, 0, "y4"), (y, 0, "acc4")], "l3b": [(xn, 0, "out")]}[kind]

        def groups(eng, body):
            for u in range(2):
                body(0, u, u, True)
            with eng.Fori(1, NG // 2) as i:
                for u in range(2):
                    body(i, u, i * 2 + u, False)

        with nc.Block() as block:
            @block.sync
            def _(sp):
                def body(i, u, g, first):
                    if not first:
                        if has_x:
                            sp.wait_ge(s_x, g - 1)
                        if has_ln:
                            sp.wait_ge(s_h, g - 1)
                    for k, (name, w) in enumerate(ins):
                        sp.dma_start(src[k][u][:, :, :], blocks_of(T[name], g * (GB * P), GB, w)).then_inc(s_ld[u], 16)

                groups(sp, body)

            @block.gpsimd
            def _(pool):
                def body(i, u, g, first):
                    if has_x:
                        pool.wait_ge(s_x, g + 1)
                    if has_ln:
                        pool.wait_ge(s_h, g + 1)
                    if has_mm:
                        pool.wait_ge(s_y, g + 1)
                    for buf, lo, name in stores:
                        pool.dma_start(blocks_of(T[name], g * (GB * P), GB), buf[u][:, :, lo:lo + D]
                                       ).then_inc(s_st[u], 16)

                groups(pool, body)
                for u in range(2):
                    pool.wait_ge(s_st[u], NG // 2 * 16 * len(stores))

            @block.vector
            def _(dve):
                def combine(i, u, g, first):
                    dve.wait_ge(s_ld[u], (i + 1) * (16 * len(ins)))
                    if not first:
                        dve.wait_ge(s_st[u], i * (16 * len(stores)))
                    if kind == "l0":
                        nc.vector.tensor_copy(S["wdst"][:, bass.ds(g * GB, GB)], src[1][u][:, :, D + 1])
                        nc.vector.tensor_scalar(small[u][:, :, 0], src[1][u][:, :, D], 1.0, None,
                                                ALU.max).then_inc(s_deg, 1)
                        dve.wait_ge(s_deg, g * 2 + 1)
                        nc.vector.reciprocal(small[u][:, :, 1], small[u][:, :, 0]).then_inc(s_deg, 1)
                        dve.wait_ge(s_deg, g * 2 + 2)
                        for j in range(GB):
                            last = nc.vector.scalar_tensor_tensor(
                                out=xn[u][:, j], in0=src[1][u][:, j, 0:D], scalar=small[u][:, j, 1:2],
                                in1=src[0][u][:, j], op0=ALU.mult, op1=ALU.add)
                        last.then_inc(s_x, 1)
                    elif kind in ("l3a", "l3b"):
                        bias = S["b31"] if kind == "l3a" else S["b32"]
                        for j in range(GB):
                            last = nc.vector.scalar_tensor_tensor(
                                out=h[u][:, j], in0=src[0][u][:, j], scalar=S["dis"][:, bass.ds(g * GB + j, 1)],
                                in1=bias[:, :], op0=ALU.mult, op1=ALU.add)
                        last.then_inc(s_deg, 1)
                        dve.wait_ge(s_deg, g + 1)
                        if kind == "l3a":
                            nc.vector.tensor_scalar(xn[u][:, :, :], h[u][:, :, :], 0.0, None, ALU.max).then_inc(s_x, 1)
                        else:
                            nc.vector.tensor_tensor(xn[u][:, :, :], h[u][:, :, :], src[1][u][:, :, :],
                                                    ALU.add).then_inc(s_x, 1)
                    elif kind == "in":
                        nc.vector.tensor_tensor(xn[u][:, :, :], src[0][u][:, :, :],
                                                S["b0"][:, :].unsqueeze(1).to_broadcast((P, GB, D)),
                                                ALU.add).then_inc(s_x, 1)
                    if has_ln:
                        if kind == "l0":
                            dve.wait_ge(s_x, g + 1)
                        sm = small[u]
                        for j in range(GB):
                            last = nc.vector.bn_stats(sm[:, j, 2:8], plain[u][:, j])
                        last.then_inc(s_bn, 1)
                        dve.wait_ge(s_bn, g * 3 + 1)
                        nc.vector.tensor_tensor(sm[:, :, 8], sm[:, :, 3], sm[:, :, 6], ALU.add)
                        nc.vector.tensor_tensor(sm[:, :, 9], sm[:, :, 3], sm[:, :, 6], ALU.subtract)
                        nc.vector.tensor_tensor(sm[:, :, 10], sm[:, :, 4], sm[:, :, 7], ALU.add).then_inc(s_bn, 1)
                        dve.wait_ge(s_bn, g * 3 + 2)
                        nc.vector.scalar_tensor_tensor(out=sm[:, :, 11], in0=sm[:, :, 9], scalar=D / 4.0,
                                                       in1=sm[:, :, 9], op0=ALU.mult, op1=ALU.mult).then_inc(s_bn, 1)
                        dve.wait_ge(s_bn, g * 3 + 3)
                        nc.vector.tensor_tensor(sm[:, :, 12], sm[:, :, 10], sm[:, :, 11], ALU.add).then_inc(s_var, 1)

                def normalise(i, u, g):
                    sm = small[u]
                    dve.wait_ge(s_std, g + 1)
                    nc.vector.reciprocal(sm[:, :, 14], sm[:, :, 13]).then_inc(s_rs, 1)
                    dve.wait_ge(s_rs, g + 1)
                    nc.vector.scalar_tensor_tensor(out=sm[:, :, 15], in0=sm[:, :, 8], scalar=-0.5, in1=sm[:, :, 14],
                                                   op0=ALU.mult, op1=ALU.mult).then_inc(s_nm, 1)

                def leave(i, u, g):
                    dve.wait_ge(s_mm, g + 1)
                    if kind in ("l2", "l3a"):
                        for j in range(GB):
                            last = nc.vector.tensor_scalar(y[u][:, j], psY[u][:, j],
                                                           S["dis"][:, bass.ds(g * GB + j, 1)], None, ALU.mult)
                    elif kind == "in":
                        nc.vector.tensor_copy(y[u][:, :, 0:D], psY[u][:, :, 0:D])
                        last = nc.vector.tensor_tensor(y[u][:, :, D:2 * D], psY[u][:, :, D:2 * D], xn[u][:, :, :],
                                                       ALU.add)
                    else:
                        last = nc.vector.tensor_copy(y[u][:, :, :], psY[u][:, :, :])
                    last.then_inc(s_y, 1)

                def body(i, u, g, first):
                    combine(i, u, g, first)
                    if has_ln:
                        normalise(i, u, g)
                    if has_mm and not (first and u == 0):
                        leave(i, 1 - u, g - 1)

                groups(dve, body)
                if has_mm:
                    leave(NG // 2 - 1, 1, NG - 1)

            @block.scalar
            def _(act):
                def body(i, u, g, first):
                    if has_ln:
                        act.wait_ge(s_var, g + 1)
                        nc.scalar.activation(small[u][:, :, 13], small[u][:, :, 12], ACT.Sqrt, bias=S["eps"][:, :],
                                             scale=1.0 / D).then_inc(s_std, 1)
                        act.wait_ge(s_nm, g + 1)
                        for j in range(GB):
                            last = nc.scalar.activation(h[u][:, j], plain[u][:, j], ACT.Relu,
                                                        bias=small[u][:, j, 15:16], scale=small[u][:, j, 14:15])
                        last.then_inc(s_h, 1)
                    if has_mm:
                        act.wait_ge(s_T, g + 1)
                        nc.scalar.copy(hT[u][:, :, :], psT[u][:, :, :]).then_inc(s_hT, 1)

                groups(act, body)

            @block.tensor
            def _(pe):
                left = h if has_ln else xn

                def body(i, u, g, first):
                    pe.wait_ge(s_h if has_ln else s_x, g + 1)
                    if not first:
                        pe.wait_ge(s_hT, g - 1)
                    for j in range(GB):
                        last = nc.tensor.transpose(psT[u][:, j], left[u][:, j], S["ident"][:, :])
                    last.then_inc(s_T, 1)
                    pe.wait_ge(s_hT, g + 1)
                    if not first:
                        pe.wait_ge(s_y, g - 1)
                    for j in range(GB):
                        if kind == "in":
                            nc.tensor.matmul(psY[u][:, j, 0:D], hT[u][:, j], S["w0n"][:, :], start=True, stop=True)
                            last = nc.tensor.matmul(psY[u][:, j, D:2 * D], hT[u][:, j], S["w0s"][:, :],
                                                    start=True, stop=True)
                        else:
                            last = nc.tensor.matmul(psY[u][:, j], hT[u][:, j], weight[:, :], start=True, stop=True)
                    last.then_inc(s_mm, 1)

                if has_mm:
                    groups(pe, body)


def gru_pass(nc, S, T, NBLK):
    PAIR = 2
    NP2 = NBLK // PAIR
    with ExitStack() as ctx:
        m = Memory(nc, ctx)
        two = range(2)
        x2 = [m.sb(f"gru_x2_{u}", [P, PAIR, D]) for u in two]
        hh = [m.sb(f"gru_h_{u}", [P, PAIR, D]) for u in two]
        a1 = [m.sb(f"gru_in_sums{u}", [P, PAIR, D]) for u in two]
        a2 = [m.sb(f"gru_out_sums{u}", [P, PAIR, D + 1]) for u in two]
        n1 = [m.sb(f"gru_neigh1_{u}", [P, PAIR, D]) for u in two]
        n2 = [m.sb(f"gru_neigh2_{u}", [P, PAIR, D]) for u in two]
        sm = [m.sb(f"gru_small{u}", [P, PAIR, 4]) for u in two]
        left = [m.sb(f"gru_left{u}", [P, PAIR, 3, D]) for u in two]
        gate = [m.sb(f"gru_gates{u}", [P, PAIR, 4 * D]) for u in two]
        th = [m.sb(f"gru_tanh{u}", [P, PAIR, 2 * D]) for u in two]
        t1 = [m.sb(f"gru_t1_{u}", [P, PAIR, D]) for u in two]
        t2 = [m.sb(f"gru_t2_{u}", [P, PAIR, D]) for u in two]
        cand = [m.sb(f"gru_cand{u}", [P, PAIR, D]) for u in two]
        x3 = [m.sb(f"gru_x3_{u}", [P, PAIR, D]) for u in two]
        pos = m.sb("gru_pos", [P, NBLK])
        safe = m.sb("gru_safe", [P, NBLK])
        gbias = m.sb("gru_bias", [P, 4 * D])
        psT = [m.ps(f"gru_psT{u}", [P, PAIR, 4, D]) for u in two]
        psG = [m.ps(f"gru_psG{u}", [P, PAIR, 4 * D]) for u in two]
        s_ld = [m.sem(f"gru_loaded{u}") for u in two]
        s_st = [m.sem(f"gru_stored{u}") for u in two]
        s_pre = m.sem("gru_scales_step")
        s_rt = m.sem("gru_dis_root")
        s_sm = m.sem("gru_small_step")
        s_n = m.sem("gru_neighbours_ready")
        s_T = m.sem("gru_transposed")
        s_L = m.sem("gru_left_ready")
        s_mm = m.sem("gru_products_ready")
        s_g = m.sem("gru_gates_ready")
        s_th = m.sem("gru_rz_ready")
        s_q = m.sem("gru_candidate_step")
        s_c = m.sem("gru_candidate_ready")
        s_x = m.sem("gru_state_step")

        def pairs(eng, body):
            for u in two:
                body(0, u, u, True)
            with eng.Fori(1, NP2 // 2) as i:
                for u in two:
                    body(i, u, i * 2 + u, False)

        with nc.Block() as block:
            @block.sync
            def _(sp):
                def body(i, u, g, first):
                    if not first:
                        sp.wait_ge(s_x, g * 3 - 3)
                    for buf, name, w in ((x2, "acc1", D), (hh, "h2", D), (a1, "acc2", D), (a2, "acc2b", D + 1)):
                        sp.dma_start(buf[u][:, :, :], blocks_of(T[name], g * (PAIR * P), PAIR, w)).then_inc(s_ld[u], 16)

                pairs(sp, body)

            @block.gpsimd
            def _(pool):
                def body(i, u, g, first):
                    pool.wait_ge(s_x, g * 3 + 3)
                    pool.dma_start(blocks_of(T["x3"], g * (PAIR * P), PAIR), x3[u][:, :, :]).then_inc(s_st[u], 16)

                pairs(pool, body)
                for u in two:
                    pool.wait_ge(s_st[u], NP2 // 2 * 16)

            @block.vector
            def _(dve):
                steps = [0]

                def link(ins):
                    steps[0] += 1
                    ins.then_inc(s_pre, 1)
                    dve.wait_ge(s_pre, steps[0])

                for shift, out in ((1.0, S["dis"]), (0.0, S["rdst"])):
                    link(nc.vector.tensor_scalar(pos[:, :], S["wdst"][:, :], shift, 0.0, ALU.add, ALU.is_gt))
                    link(nc.vector.tensor_scalar(safe[:, :], S["wdst"][:, :], shift - 1.0, None, ALU.add))
                    link(nc.vector.tensor_tensor(safe[:, :], safe[:, :], pos[:, :], ALU.mult))
                    link(nc.vector.tensor_scalar(safe[:, :], safe[:, :], 1.0, None, ALU.add))
                    link(nc.vector.reciprocal(safe[:, :], safe[:, :]))
                    link(nc.vector.tensor_tensor(out[:, :], safe[:, :], pos[:, :], ALU.mult))
                nc.vector.tensor_tensor(gbias[:, 0:2 * D], S["bih"][:, 0:2 * D], S["bhh"][:, 0:2 * D], ALU.add)
                nc.vector.tensor_copy(gbias[:, 2 * D:3 * D], S["bih"][:, 2 * D:3 * D])
                link(nc.vector.tensor_copy(gbias[:, 3 * D:4 * D], S["bhh"][:, 2 * D:3 * D]))

                def means(i, u, g, first):
                    dve.wait_ge(s_ld[u], i * 64 + 64)
                    w = a2[u][:, :, D]
                    nc.vector.tensor_scalar(sm[u][:, :, 0], w, 0.0, None, ALU.is_gt)
                    nc.vector.tensor_scalar(sm[u][:, :, 1], w, -1.0, None, ALU.add).then_inc(s_sm, 1)
                    for j in range(PAIR):
                        nc.vector.tensor_scalar(n1[u][:, j], a1[u][:, j], S["rdst"][:, bass.ds(g * PAIR + j, 1)],
                                                None, ALU.mult)
                    dve.wait_ge(s_sm, g * 5 + 1)
                    nc.vector.tensor_tensor(sm[u][:, :, 2], sm[u][:, :, 0], sm[u][:, :, 1], ALU.mult).then_inc(s_sm, 1)
                    dve.wait_ge(s_sm, g * 5 + 2)
                    nc.vector.tensor_scalar(sm[u][:, :, 1], sm[u][:, :, 2], 1.0, None, ALU.add).then_inc(s_sm, 1)
                    dve.wait_ge(s_sm, g * 5 + 3)
                    nc.vector.reciprocal(sm[u][:, :, 2], sm[u][:, :, 1]).then_inc(s_sm, 1)
                    dve.wait_ge(s_sm, g * 5 + 4)
                    nc.vector.tensor_tensor(sm[u][:, :, 3], sm[u][:, :, 2], sm[u][:, :, 0], ALU.mult).then_inc(s_sm, 1)
                    dve.wait_ge(s_sm, g * 5 + 5)
                    for j in range(PAIR):
                        last = nc.vector.tensor_scalar(n2[u][:, j], a2[u][:, j, 0:D], sm[u][:, j, 3:4], None, ALU.mult)
                    last.then_inc(s_n, 1)

                def gates(i, u, g):
                    dve.wait_ge(s_mm, g + 1)
                    nc.vector.tensor_tensor(gate[u][:, :, :], psG[u][:, :, :],
                                            gbias[:, :].unsqueeze(1).to_broadcast((P, PAIR, 4 * D)),
                                            ALU.add).then_inc(s_g, 1)

                def state(i, u, g, first):
                    dve.wait_ge(s_th, g + 1)
                    nc.vector.scalar_tensor_tensor(out=t1[u][:, :, :], in0=th[u][:, :, 0:D], scalar=1.0,
                                                   in1=gate[u][:, :, 3 * D:4 * D], op0=ALU.add,
                                                   op1=ALU.mult).then_inc(s_q, 1)
                    dve.wait_ge(s_q, g * 2 + 1)
                    nc.vector.scalar_tensor_tensor(out=t2[u][:, :, :], in0=t1[u][:, :, :], scalar=0.5,
                                                   in1=gate[u][:, :, 2 * D:3 * D], op0=ALU.mult,
                                                   op1=ALU.add).then_inc(s_q, 1)

                def finish(i, u, g, first):
                    dve.wait_ge(s_c, g + 1)
                    if not first:
                        dve.wait_ge(s_st[u], i * 16)
                    nc.vector.tensor_tensor(x3[u][:, :, :], x2[u][:, :, :], cand[u][:, :, :], ALU.add)
                    nc.vector.tensor_tensor(t1[u][:, :, :], hh[u][:, :, :], cand[u][:, :, :],
                                            ALU.subtract).then_inc(s_x, 1)
                    dve.wait_ge(s_x, g * 3 + 1)
                    nc.vector.scalar_tensor_tensor(out=t2[u][:, :, :], in0=th[u][:, :, D:2 * D], scalar=1.0,
                                                   in1=t1[u][:, :, :], op0=ALU.add, op1=ALU.mult).then_inc(s_x, 1)
                    dve.wait_ge(s_x, g * 3 + 2)
                    nc.vector.scalar_tensor_tensor(out=x3[u][:, :, :], in0=t2[u][:, :, :], scalar=0.5,
                                                   in1=x3[u][:, :, :], op0=ALU.mult, op1=ALU.add).then_inc(s_x, 1)

                def body(i, u, g, first):
                    means(i, u, g, first)
                    if not (first and u == 0):
                        state(i, 1 - u, g - 1, False)
                    gates(i, u, g)
                    if not (first and u == 0):
                        finish(i if u else i - 1, 1 - u, g - 1, first)

                pairs(dve, body)
                state(NP2 // 2 - 1, 1, NP2 - 1, False)
                finish(NP2 // 2 - 1, 1, NP2 - 1, False)

            @block.scalar
            def _(act):
                act.wait_ge(s_pre, 6)
                nc.scalar.activation(S["dis"][:, :], S["dis"][:, :], ACT.Sqrt).then_inc(s_rt, 1)

                def candidate(i, u, g):
                    act.wait_ge(s_q, g * 2 + 2)
                    nc.scalar.activation(cand[u][:, :, :], t2[u][:, :, :], ACT.Tanh).then_inc(s_c, 1)

                def body(i, u, g, first):
                    act.wait_ge(s_T, g + 1)
                    nc.scalar.copy(left[u][:, :, :, :], psT[u][:, :, 0:3, :]).then_inc(s_L, 1)
                    if not (first and u == 0):
                        candidate(i, 1 - u, g - 1)
                    act.wait_ge(s_g, g + 1)
                    nc.scalar.activation(th[u][:, :, :], gate[u][:, :, 0:2 * D], ACT.Tanh, scale=0.5).then_inc(s_th, 1)

                pairs(act, body)
                candidate(NP2 // 2 - 1, 1, NP2 - 1)

            @block.tensor
            def _(pe):
                def body(i, u, g, first):
                    pe.wait_ge(s_n, g + 1)
                    if not first:
                        pe.wait_ge(s_L, g - 1)
                    for j in range(PAIR):
                        for k, part in enumerate((n1, n2, hh)):
                            last = nc.tensor.transpose(psT[u][:, j, k], part[u][:, j], S["ident"][:, :])
                    last.then_inc(s_T, 1)
                    pe.wait_ge(s_L, g + 1)
                    if not first:
                        pe.wait_ge(s_g, g - 1)
                    for j in range(PAIR):
                        nc.tensor.matmul(psG[u][:, j, 0:3 * D], left[u][:, j, 0], S["wih"][:, 0, :], start=True,
                                         stop=False, skip_group_check=True)
                        nc.tensor.matmul(psG[u][:, j, 0:3 * D], left[u][:, j, 1], S["wih"][:, 1, :], start=False,
                                         stop=False, skip_group_check=True)
                        nc.tensor.matmul(psG[u][:, j, 0:2 * D], left[u][:, j, 2], S["whh"][:, 0:2 * D], start=False,
                                         stop=True, skip_group_check=True)
                        last = nc.tensor.matmul(psG[u][:, j, 3 * D:4 * D], left[u][:, j, 2], S["whh"][:, 2 * D:3 * D],
                                                start=True, stop=True, skip_group_check=True)
                    last.then_inc(s_mm, 1)

                pairs(pe, body)


def message_pass(nc, A, S, T, NT, X):
    STEPS = NT // RING
    ring, comb, eq, row, bank = X["ring"], X["comb"], X["eq"], X["row"], X["bank"]
    gslot, sslot = X["gslot"], X["sslot"]
    s_gath, s_row, s_eq = X["s_gath"], X["s_row"], X["s_eq"]
    s_mm, s_ev, s_scat, s_gidx, s_sidx = X["s_mm"], X["s_ev"], X["s_scat"], X["s_gidx"], X["s_sidx"]
    s_go = X["s_go"]
    gidx, sidx = S["srci"], S["dstu"]
    table, acc = T["y1"], T["acc1"]
    W4 = GB * P
    with ExitStack() as ctx:
        m = Memory(nc, ctx)
        two = range(2)
        rad = [m.sb(f"m_radius{h}", [NBASIS, W4]) for h in two]
        clip = m.sb("m_clipped", [NBASIS, W4])
        keep = m.sb("m_inside", [NBASIS, W4])
        sq = m.sb("m_square", [NBASIS, W4])
        ex = m.sb("m_gauss", [NBASIS, W4])
        emb = m.sb("m_embedding", [NBASIS, W4])
        th = m.sb("m_tanh", [HID, W4])
        z = m.sb("m_z", [HID, W4])
        hid1 = m.sb("m_hidden1", [HID, W4])
        mid = [m.sb(f"m_mid{h}", [P, GB, 2 * D]) for h in two]
        t1 = m.sb("m_w1s", [P, GB, MUL])
        dots = m.sb("m_products", [P, GB, 3, MUL])
        dot = m.sb("m_dot", [P, GB, MUL])
        dot2 = m.sb("m_dot2", [P, GB, MUL])
        midT = m.sb("m_sumsT", [P, 2, 2, P])
        psH = m.ps("m_psH", [HID, W4])
        psW = m.ps("m_psW", [P, GB, D])
        s_rad = [m.sem(f"m_radius_loaded{h}") for h in two]
        s_clip = m.sem("m_clipped")
        s_spgo = m.sem("m_sync_waits_passed")
        s_pego = m.sem("m_tensor_waits_passed")
        s_sq = m.sem("m_squared")
        s_gauss = m.sem("m_gauss_ready")
        s_emb = m.sem("m_embedding_ready")
        s_h = m.sem("m_hidden_product")
        s_th = m.sem("m_tanh_ready")
        s_hid = m.sem("m_hidden_ready")
        s_w = m.sem("m_radial_weights")
        s_msg = m.sem("m_message_step")
        s_T = m.sem("m_sumsT_product")
        s_Tc = m.sem("m_sumsT_ready")
        MS = 6

        def steps(eng, body):
            for h in two:
                body(0, h, h, True, False)
            with eng.Fori(1, STEPS - 1) as i:
                for h in two:
                    body(i, h, i * 2 + h, False, False)
            for h in two:
                body(STEPS - 1, h, (STEPS - 1) * 2 + h, False, h == 1)

        with nc.Block() as block:
            @block.sync
            def _(sp):
                def body(i, h, n, first, last):
                    if not first:
                        sp.wait_ge(s_eq, n * GB - GB)
                        sp.sem_inc(s_spgo, 1)
                        sp.wait_ge(s_clip, n - 1)
                        sp.sem_inc(s_spgo, 1)
                    sp.dma_start(rad[h][:, :], row_of(A["edge_weight"], n * W4, W4, NBASIS)).then_inc(s_rad[h], 16)
                    sp.dma_start(row[h][:, :], row_of(A["dst"], n * W4, W4, P)).then_inc(s_row[h], 16)

                steps(sp, body)

            @block.gpsimd
            def _(pool):
                def gather(i, h, n, j, first):
                    t = n * GB + j
                    if j == 0:
                        if not first:
                            pool.wait_ge(s_mm, t - GB)
                        nc.gpsimd.tensor_copy(gslot[:, h * GB:(h + 1) * GB],
                                              gidx[:, bass.ds(t, GB)]).then_inc(s_gidx, 1)
                        pool.wait_ge(s_gidx, n + 1)
                        if not first:
                            pool.wait_ge(s_msg, n * MS - MS)
                    slot = h * GB + j
                    pool.sem_inc(s_go, 1)
                    pool.indirect_dma_start(ring[:, slot, :], None, table[:, :],
                                            bass.IndirectOffsetOnAxis(ap=gslot[:, slot:slot + 1], axis=0)
                                            ).then_inc(s_gath[slot], 16)

                def scatter(i, h, n, j, first, refill=True):
                    t, slot = n * GB + j - GB, (1 - h) * GB + j
                    started = not (first and h == 0)
                    if started and not (first and j == 0):
                        pool.wait_ge(s_scat, t * 16)
                    if j == 0 and refill:
                        nc.gpsimd.tensor_copy(sslot[:, h * GB:(h + 1) * GB],
                                              sidx[:, bass.ds(t + GB, GB)]).then_inc(s_sidx, 1)
                    if started:
                        if j == 0:
                            pool.wait_ge(s_sidx, n)
                        pool.wait_ge(s_ev, t + 1)
                        pool.sem_inc(s_go, 1)
                        pool.indirect_dma_start(acc[:, :],
                                                bass.IndirectOffsetOnAxis(ap=sslot[:, slot:slot + 1], axis=0),
                                                comb[:, slot, 0:D], None, compute_op=ALU.add).then_inc(s_scat, 16)

                def body(i, h, n, first, last):
                    for j in range(GB):
                        gather(i, h, n, j, first)
                    for j in range(GB):
                        scatter(i, h, n, j, first)

                steps(pool, body)
                for j in range(GB):
                    scatter(STEPS, 0, STEPS * 2, j, False, refill=False)
                pool.wait_ge(s_scat, NT * 16)

            @block.vector
            def _(dve):
                def radial_head(i, h, n):
                    dve.wait_ge(s_rad[h], i * 16 + 16)
                    nc.vector.tensor_scalar(keep[:, :], rad[h][:, :], 1.0, float(NBASIS) ** 0.5, ALU.is_le, ALU.mult)
                    nc.vector.tensor_scalar(clip[:, :], rad[h][:, :], 0.0, 1.0, ALU.max, ALU.min).then_inc(s_clip, 1)

                def embed(n):
                    dve.wait_ge(s_gauss, n + 1)
                    nc.vector.tensor_tensor(emb[:, :], ex[:, :], keep[:, :], ALU.mult).then_inc(s_emb, 1)

                def hidden(n, layer, out):
                    dve.wait_ge(s_th, n * 2 + layer + 1)
                    nc.vector.scalar_tensor_tensor(out=out, in0=th[:, :], scalar=1.0, in1=z[:, :], op0=ALU.add,
                                                   op1=ALU.mult).then_inc(s_hid, 1)

                def equal(i, h, n, first):
                    dve.wait_ge(s_row[h], i * 16 + 16)
                    for j in range(GB):
                        t = n * GB + j
                        if not (first and h == 0):
                            dve.wait_ge(s_mm, t - GB + 1)
                        nc.vector.tensor_scalar(eq[:, j, :], row[h][:, j * P:(j + 1) * P],
                                                S["dstf"][:, bass.ds(t, 1)], None, ALU.is_equal).then_inc(s_eq, 1)

                def messages(i, h, n, first):
                    g = ring[:, h * GB:(h + 1) * GB, :]
                    s = g[:, :, 0:MUL]
                    v = g[:, :, MUL:D].rearrange("p j (c k) -> p j c k", c=3)
                    w = [psW[:, :, k * MUL:(k + 1) * MUL] for k in range(4)]
                    out = mid[h]
                    unit = S["rhat"][:, bass.ds(n * GB, GB), :].unsqueeze(3).to_broadcast((P, GB, 3, MUL))
                    y1 = S["y1c"][:, bass.ds(n * GB, GB), :].unsqueeze(3).to_broadcast((P, GB, 3, MUL))
                    for j in range(GB):
                        dve.wait_ge(s_gath[h * GB + j], i * 16 + 16)
                    if not first:
                        dve.wait_ge(s_mm, n * GB - GB)
                    nc.vector.tensor_tensor(dots[:, :, :, :], v, unit, ALU.mult).then_inc(s_msg, 1)
                    dve.wait_ge(s_w, n + 1)
                    nc.vector.tensor_tensor(t1[:, :, :], w[1], s, ALU.mult).then_inc(s_msg, 1)
                    nc.vector.tensor_tensor(out[:, :, 0:MUL], w[0], s, ALU.mult)
                    dve.wait_ge(s_msg, n * MS + 1)
                    nc.vector.tensor_tensor(dot[:, :, :], dots[:, :, 0, :], dots[:, :, 1, :], ALU.add).then_inc(s_msg, 1)
                    dve.wait_ge(s_msg, n * MS + 2)
                    nc.vector.tensor_tensor(out[:, :, 2 * MUL:5 * MUL].rearrange("p j (c k) -> p j c k", c=3),
                                            t1[:, :, :].unsqueeze(2).to_broadcast((P, GB, 3, MUL)), y1, ALU.mult)
                    dve.wait_ge(s_msg, n * MS + 3)
                    nc.vector.tensor_tensor(dot2[:, :, :], dot[:, :, :], dots[:, :, 2, :], ALU.add).then_inc(s_msg, 1)
                    nc.vector.tensor_tensor(out[:, :, 5 * MUL:8 * MUL].rearrange("p j (c k) -> p j c k", c=3),
                                            w[2].unsqueeze(2).to_broadcast((P, GB, 3, MUL)), v,
                                            ALU.mult).then_inc(s_msg, 1)
                    dve.wait_ge(s_msg, n * MS + 4)
                    nc.vector.tensor_tensor(out[:, :, MUL:2 * MUL], w[3], dot2[:, :, :], ALU.mult).then_inc(s_msg, 1)

                hid2 = S["hid2"][0:HID, 0, :]

                def body(i, h, n, first, last):
                    equal(i, h, n, first)
                    if not last:
                        radial_head(i if h == 0 else i + 1, 1 - h, n + 1)
                    messages(i, h, n, first)
                    if not last:
                        embed(n + 1)
                        hidden(n + 1, 0, hid1[:, :])
                        hidden(n + 1, 1, hid2)

                radial_head(0, 0, 0)
                embed(0)
                hidden(0, 0, hid1[:, :])
                hidden(0, 1, hid2)
                steps(dve, body)

            @block.scalar
            def _(act):
                def radial(n):
                    act.wait_ge(s_clip, n + 1)
                    nc.scalar.activation(sq[:, :], clip[:, :], ACT.Square, bias=S["ncen"][:, :],
                                         scale=float(NBASIS - 1)).then_inc(s_sq, 1)
                    act.wait_ge(s_sq, n + 1)
                    nc.scalar.activation(ex[:, :], sq[:, :], ACT.Exp, scale=-0.5).then_inc(s_gauss, 1)
                    for layer, bias in ((0, S["mb0"]), (1, S["mb1"])):
                        act.wait_ge(s_h, n * 2 + layer + 1)
                        nc.scalar.activation(z[:, :], psH[:, :], ACT.Identity, bias=bias[:, 0:1])
                        nc.scalar.activation(th[:, :], psH[:, :], ACT.Tanh, bias=bias[:, 1:2],
                                             scale=0.5).then_inc(s_th, 1)

                def body(i, h, n, first, last):
                    for j in range(GB):
                        t = n * GB + j
                        act.wait_ge(s_T, t + 1)
                        nc.scalar.copy(midT[:, j % 2], bank[j % 2][:, 0:2 * P].rearrange("p (k e) -> p k e", k=2)
                                       ).then_inc(s_Tc, 1)
                        act.wait_ge(s_mm, t + 1)
                        if not first:
                            act.wait_ge(s_scat, (t - RING + 1) * 16)
                        nc.scalar.copy(comb[:, h * GB + j, 0:D], bank[2 + j % 2][:, 0:D]).then_inc(s_ev, 1)
                    if not last:
                        radial(n + 1)

                radial(0)
                steps(act, body)

            @block.tensor
            def _(pe):
                def radial(n):
                    pe.wait_ge(s_emb, n + 1)
                    nc.tensor.matmul(psH[:, :], S["mw0"][:, :], emb[:, :], start=True, stop=True).then_inc(s_h, 1)
                    pe.wait_ge(s_hid, n * 2 + 1)
                    pe.sem_inc(s_pego, 1)
                    nc.tensor.matmul(psH[:, :], S["mw1"][:, :], hid1[:, :], start=True, stop=True).then_inc(s_h, 1)
                    pe.wait_ge(s_hid, n * 2 + 2)

                def body(i, h, n, first, last):
                    if not first or h == 1:
                        pe.wait_ge(s_msg, n * MS)
                    for j in range(GB):
                        mm = nc.tensor.matmul(psW[:, j, :], S["hid2"][:, 0, j * P:(j + 1) * P], S["mw2"][:, :],
                                              start=True, stop=True)
                    mm.then_inc(s_w, 1)
                    pe.wait_ge(s_msg, (n + 1) * MS)
                    for j in range(GB):
                        t = n * GB + j
                        pe.wait_ge(s_eq, t + 1)
                        if not (first and h == 0 and j < 2):
                            pe.wait_ge(s_Tc, t - 1)
                        for k in range(2):
                            mm = nc.tensor.matmul(bank[j % 2][:, k * P:(k + 1) * P], mid[h][:, j, k * D:(k + 1) * D],
                                                  eq[:, j, :], start=True, stop=True)
                        mm.then_inc(s_T, 1)
                        pe.wait_ge(s_Tc, t + 1)
                        if not (first and h == 0 and j < 2):
                            pe.wait_ge(s_ev, t - 1)
                        for k in range(2):
                            mm = nc.tensor.matmul(bank[2 + j % 2][:, 0:D], midT[:, j % 2, k, :], S["wout"][:, k, :],
                                                  start=k == 0, stop=k == 1)
                        mm.then_inc(s_mm, 1)
                    if not last:
                        radial(n + 1)

                radial(0)
                steps(pe, body)


def program(nc, A, out):
    NP = out.shape[0]
    NE = A["src"].shape[0]
    NT, NBLK = NE // P, NP // P
    T = {"x": A["x"], "out": out}
    for name, width, spare in (("own", D, 0), ("y0", D, 0), ("acc0", D + 2, P), ("y1", D, 0), ("acc1", D, P),
                               ("h2", D, 0), ("acc2", D, P), ("acc2b", D + 1, P), ("x3", D, 0), ("y3", D, 0),
                               ("acc3", D, P), ("y4", D, 0), ("acc4", D, P)):
        T[name] = nc.dram_tensor(f"t_{name}", (NP + spare, width), f32, kind="Internal").ap()
    with ExitStack() as ctx:
        m = Memory(nc, ctx)
        S = {}
        for name, shape in (("part", [P, 1]), ("ident", [P, P]), ("earlier", [P, P]), ("spare", [P, 1]),
                            ("ncen", [NBASIS, 1]), ("eps", [P, 1]), ("srcf", [P, NT]), ("dstf", [P, NT]),
                            ("w", [P, NT]), ("onew", [P, NT, 2]), ("rhat", [P, NT, 3]), ("y1c", [P, NT, 3]),
                            ("w0s", [P, D]), ("w0n", [P, D]), ("b0", [P, D]), ("wup", [P, D]), ("wout", [P, 2, D]),
                            ("mw0", [NBASIS, HID]), ("mw1", [HID, HID]), ("mw2", [HID + 1, D]), ("mb0", [HID, 2]),
                            ("mb1", [HID, 2]), ("hid2", [HID + 1, 1, GB * P]), ("wih", [P, 2, 3 * D]),
                            ("whh", [P, 3 * D]), ("bih", [P, 3 * D]), ("bhh", [P, 3 * D]), ("w31", [P, D]),
                            ("w32", [P, D]), ("b31", [P, D]), ("b32", [P, D]), ("wdst", [P, NBLK]),
                            ("rdst", [P, NBLK]), ("dis", [P, NBLK])):
            S[name] = m.sb(name, shape)
        for name in ("srci", "dsti", "srcu", "dstu"):
            S[name] = m.sb(name, [P, NT], i32)

        setup_pass(nc, A, S, T, NT, NP)
        unique_pass(nc, A, S, NT)
        node_pass(nc, S, T, NBLK // GB, "in")

        def edges(tag, make, *args):
            with ExitStack() as inner:
                e = Memory(nc, inner)
                X = {"s_gath": [e.sem(f"{tag}_row_gathered{j}") for j in range(RING)],
                     "s_row": [e.sem(f"{tag}_targets_loaded{h}") for h in range(2)], "s_eq": e.sem(f"{tag}_equality_built"),
                     "s_mm": e.sem(f"{tag}_tile_summed"), "s_ev": e.sem(f"{tag}_tile_sums_ready"), "s_scat": e.sem(f"{tag}_tile_added"),
                     "s_go": e.sem(f"{tag}_pool_waits_passed"), "s_gidx": e.sem(f"{tag}_gather_indices_ready"),
                     "s_sidx": e.sem(f"{tag}_scatter_indices_ready")}
                X["ring"] = e.sb(f"{tag}_ring", [P, RING, D])
                X["comb"] = e.sb(f"{tag}_tile_sums", [P, RING, D + 2])
                X["eq"] = e.sb(f"{tag}_equal", [P, GB, P])
                X["row"] = [e.sb(f"{tag}_targets{h}", [P, GB * P], i32) for h in range(2)]
                X["gslot"] = e.sb(f"{tag}_gather_slots", [P, RING], i32)
                X["sslot"] = e.sb(f"{tag}_scatter_slots", [P, RING], i32)
                X["bank"] = [e.ps(f"{tag}_sums{j}", [P, 512]) for j in range(GB)]
                make(nc, A, S, T, NT, X, *args)

        edges("l0", edge_pass, "y0", "acc0", "src", "dst", False, "deg")
        node_pass(nc, S, T, NBLK // GB, "l0")
        edges("l1", message_pass)
        node_pass(nc, S, T, NBLK // GB, "l1")
        edges("l2in", edge_pass, "h2", "acc2", "src", "dst", True, "")
        edges("l2out", edge_pass, "h2", "acc2b", "dst", "src", True, "w")
        gru_pass(nc, S, T, NBLK)
        node_pass(nc, S, T, NBLK // GB, "l2")
        edges("l3a", edge_pass, "y3", "acc3", "src", "dst", True, "")
        node_pass(nc, S, T, NBLK // GB, "l3a")
        edges("l3b", edge_pass, "y4", "acc4", "src", "dst", True, "")
        node_pass(nc, S, T, NBLK // GB, "l3b")


NAMES = ["x", "src", "dst", "edge_attr_3", "edge_weight", "L0_gnn_W", "L0_gnn_b", "L1_gnn_W_up0", "L1_gnn_W_up1",
         "L1_gnn_mlp_w0", "L1_gnn_mlp_b0", "L1_gnn_mlp_w1", "L1_gnn_mlp_b1", "L1_gnn_mlp_w2", "L1_gnn_mlp_b2",
         "L1_gnn_W_out0", "L1_gnn_W_out1", "L2_gnn_W1", "L2_gnn_W2", "L2_gnn_w_ih", "L2_gnn_w_hh", "L2_gnn_b_ih",
         "L2_gnn_b_hh", "L3_gnn_W1", "L3_gnn_b1", "L3_gnn_W2", "L3_gnn_b2"]


def padded(a, rows, fill=0):
    import numpy as np
    tail = np.full((rows - a.shape[0],) + a.shape[1:], fill, a.dtype)
    return np.concatenate([a, tail])


def layout(inputs):
    import numpy as np

    arrays = {k: np.ascontiguousarray(v) for k, v in inputs.items()}
    step = RING * P
    nodes = -(-(arrays["x"].shape[0] + 1) // step) * step
    edges = -(-arrays["src"].shape[0] // step) * step
    arrays["x"] = padded(arrays["x"], nodes)
    for name in ("src", "dst"):
        arrays[name] = padded(arrays[name], edges, nodes - 1)
    for name in ("edge_attr_3", "edge_weight"):
        arrays[name] = padded(arrays[name], edges)
    return arrays


def kernel(**inputs):
    import concourse.bacc as bacc
    from concourse.bass_utils import run_bass_kernel_spmd as run

    arrays = layout(inputs)
    nc = bacc.Bacc("TRN2", target_bir_lowering=False, num_devices=1)
    tables, feed = {}, {}
    for name in NAMES:
        feed[f"in_{name}"] = arrays[name]
        tables[name] = nc.dram_tensor(f"in_{name}", arrays[name].shape, mybir.dt.from_np(arrays[name].dtype),
                                      kind="ExternalInput").ap()
    out = nc.dram_tensor("out_x", arrays["x"].shape, f32, kind="ExternalOutput").ap()
    program(nc, tables, out)
    r = run(nc, [feed], core_ids=[0])
    return r.results[0]["out_x"][:inputs["x"].shape[0]]
```
